# Optimizing a Trainium2 kernel written in Bass

```python
import numpy as np
import jax
import jax.numpy as jnp

def _softmax(x, axis=-1):
    return jax.nn.softmax(x, axis=axis)

def _gelu(x):
    return jax.nn.gelu(x, approximate=True)

def _silu(x):
    return jax.nn.silu(x)

def _sigmoid(x):
    return jax.nn.sigmoid(x)

def _layernorm(x, axis=-1, eps=1e-05):
    m = jnp.mean(x, axis=axis, keepdims=True)
    v = jnp.var(x, axis=axis, keepdims=True)
    return (x - m) / jnp.sqrt(v + eps)

def _scatter_add(tgt, idx, src, axis=0):
    return tgt.at[idx].add(src)

def _segment_sum(src, seg, n):
    return jax.ops.segment_sum(src, seg, n)
kernel_name = 'mk_xattn_seq_d1_seqx_r2_8ccbed'

def setup_inputs(seed: int=0):
    np.random.seed(seed)
    _w = jnp.asarray

    def _rec_inputs():
        import jax
        import jax.numpy as jnp
        _rk = jax.random.key(seed)
        x = -0.0002928 + 1 * jax.random.normal(jax.random.fold_in(_rk, 1), (32, 512, 512), jnp.float32)
        _lenS = 512 - jax.random.randint(jax.random.fold_in(_rk, 7), (32,), 0, max(1, 512 // 4) + 1, jnp.int32)
        _lenS2 = 512 - jax.random.randint(jax.random.fold_in(_rk, 8), (32,), 0, max(1, 512 // 4) + 1, jnp.int32)
        _ctx_1024P = jax.random.normal(jax.random.fold_in(_rk, 11), (32, 16, 512), jnp.float32)
        _ctx_1024c = jax.random.dirichlet(jax.random.fold_in(_rk, 511), 0.3 * jnp.ones((16,), jnp.float32), (32, 512))
        _ctx_1024t = jnp.einsum('bsk,bkd->bsd', _ctx_1024c, _ctx_1024P)
        _ctx_1024t = _ctx_1024t * jax.lax.rsqrt(jnp.mean(jnp.square(_ctx_1024t)) + 1e-12) * 0.953939
        ctx_1024 = 2.81802e-05 + 1.00001 * (_ctx_1024t + 0.3 * jax.random.normal(jax.random.fold_in(_rk, 611), (32, 512, 512), jnp.float32))
        return (x, ctx_1024)
    x, ctx_1024 = _rec_inputs()

    def _L0_xattn_setup():
        import jax, jax.numpy as jnp
        import numpy as np
        D_Q = 512
        D_KV = 512
        D_ATTN = 512
        NUM_HEADS = 16
        D_HEAD = D_ATTN // NUM_HEADS

        def layer_norm(x, gamma, beta, eps=1e-05):
            mu = jnp.mean(x, axis=-1, keepdims=True)
            var = jnp.var(x, axis=-1, keepdims=True)
            return (x - mu) * jax.lax.rsqrt(var + eps) * gamma + beta
        key = jax.random.key(seed)
        ks = jax.random.split(key, 10)
        B, N_q, N_kv = (4, 512, 2048)
        s_q = 1.0 / np.sqrt(D_Q)
        s_kv = 1.0 / np.sqrt(D_KV)
        s_a = 1.0 / np.sqrt(D_ATTN)
        return {'q': jax.random.normal(ks[0], (B, N_q, D_Q), jnp.float32), 'kv': jax.random.normal(ks[1], (B, N_kv, D_KV), jnp.float32), 'q_norm_g': jnp.ones((D_Q,), jnp.float32), 'q_norm_b': jnp.zeros((D_Q,), jnp.float32), 'kv_norm_g': jnp.ones((D_KV,), jnp.float32), 'kv_norm_b': jnp.zeros((D_KV,), jnp.float32), 'Wq': jax.random.normal(ks[2], (D_Q, D_ATTN), jnp.float32) * s_q, 'Wk': jax.random.normal(ks[3], (D_KV, D_ATTN), jnp.float32) * s_kv, 'Wv': jax.random.normal(ks[4], (D_KV, D_ATTN), jnp.float32) * s_kv, 'Wo': jax.random.normal(ks[5], (D_ATTN, D_Q), jnp.float32) * s_a, 'bo': jnp.zeros((D_Q,), jnp.float32)}
    _L0_xattn_all = _L0_xattn_setup()
    _L0_xattn_in = {k: v for k, v in _L0_xattn_all.items() if k in ('q_norm_g', 'q_norm_b', 'kv_norm_g', 'kv_norm_b', 'Wq', 'Wk', 'Wv', 'Wo', 'bo')}
    del _L0_xattn_all
    return {'x': x, 'ctx_1024': ctx_1024, 'L0_xattn_q_norm_g': _L0_xattn_in['q_norm_g'], 'L0_xattn_q_norm_b': _L0_xattn_in['q_norm_b'], 'L0_xattn_kv_norm_g': _L0_xattn_in['kv_norm_g'], 'L0_xattn_kv_norm_b': _L0_xattn_in['kv_norm_b'], 'L0_xattn_Wq': _L0_xattn_in['Wq'], 'L0_xattn_Wk': _L0_xattn_in['Wk'], 'L0_xattn_Wv': _L0_xattn_in['Wv'], 'L0_xattn_Wo': _L0_xattn_in['Wo'], 'L0_xattn_bo': _L0_xattn_in['bo']}

def reference(x, ctx_1024, L0_xattn_q_norm_g, L0_xattn_q_norm_b, L0_xattn_kv_norm_g, L0_xattn_kv_norm_b, L0_xattn_Wq, L0_xattn_Wk, L0_xattn_Wv, L0_xattn_Wo, L0_xattn_bo):
    import jax
    import jax.numpy as jnp

    def _L0_xattn_ref(q, kv, q_norm_g, q_norm_b, kv_norm_g, kv_norm_b, Wq, Wk, Wv, Wo, bo):
        import jax, jax.numpy as jnp
        import numpy as np
        D_Q = 512
        D_KV = 512
        D_ATTN = 512
        NUM_HEADS = 16
        D_HEAD = D_ATTN // NUM_HEADS

        def layer_norm(x, gamma, beta, eps=1e-05):
            mu = jnp.mean(x, axis=-1, keepdims=True)
            var = jnp.var(x, axis=-1, keepdims=True)
            return (x - mu) * jax.lax.rsqrt(var + eps) * gamma + beta
        B, N_q, _ = q.shape
        N_kv = kv.shape[1]
        qn = layer_norm(q, q_norm_g, q_norm_b)
        kvn = layer_norm(kv, kv_norm_g, kv_norm_b)
        Q = (qn @ Wq).reshape(B, N_q, NUM_HEADS, D_HEAD).transpose(0, 2, 1, 3)
        K = (kvn @ Wk).reshape(B, N_kv, NUM_HEADS, D_HEAD).transpose(0, 2, 1, 3)
        V = (kvn @ Wv).reshape(B, N_kv, NUM_HEADS, D_HEAD).transpose(0, 2, 1, 3)
        scores = jnp.einsum('bhqd,bhkd->bhqk', Q, K) / jnp.sqrt(jnp.float32(D_HEAD))
        attn = jax.nn.softmax(scores, axis=-1)
        ctx = jnp.einsum('bhqk,bhkd->bhqd', attn, V)
        ctx = ctx.transpose(0, 2, 1, 3).reshape(B, N_q, D_ATTN)
        out = q + jax.nn.gelu(ctx @ Wo + bo, approximate=False)
        return out
    x = _L0_xattn_ref(x, ctx_1024, L0_xattn_q_norm_g, L0_xattn_q_norm_b, L0_xattn_kv_norm_g, L0_xattn_kv_norm_b, L0_xattn_Wq, L0_xattn_Wk, L0_xattn_Wv, L0_xattn_Wo, L0_xattn_bo)
    return x

_drawn_inputs = setup_inputs


def setup_inputs(seed=0):
    import zlib

    import numpy as np

    out = dict(_drawn_inputs(seed))
    spreads = {'L0_xattn_q_norm_g': (1.0, 0.6),
     'L0_xattn_q_norm_b': (0.0, 0.76),
     'L0_xattn_kv_norm_g': (1.0, 0.2),
     'L0_xattn_kv_norm_b': (0.0, 0.1),
     'L0_xattn_bo': (0.0, 0.1)}
    factors = {}
    for name, (base, spread) in spreads.items():
        noise = np.random.default_rng([zlib.crc32(name.encode()), seed]).standard_normal(out[name].shape)
        drawn = base * np.exp(spread * noise) if base else spread * noise
        out[name] = jnp.asarray(drawn.astype(out[name].dtype))
    for name, factor in factors.items():
        out[name] = (out[name] * factor).astype(out[name].dtype)
    return out
```

```python
from contextlib import ExitStack

import concourse.bass as bass
from concourse import mybir

ALU = mybir.AluOpType
ACT = mybir.ActivationFunctionType
AX_X = mybir.AxisListType.X
F32 = mybir.dt.float32
F32R = mybir.dt.float32r

P = 128
D = 512
NC = D // P
HEADS = 16
DH = D // HEADS
HU = P // DH
NU = HEADS // HU
KROWS = 3 * DH
SROW = KROWS
SCALE = float(DH) ** -0.5
EPS = 1e-5
NSLOT = 5
TILE_SLOT = [3, 4, 0, 1, 2, 3, 4, 0]

PARTS = 3
OVER_BATCH = ("v", "o", "gelu", "res_add", "store", "res", "load", "ln", "norm", "x")
ORDER = {
    "pe": (
        "v*5 st*2 v*3 st s st s v s st s st z st s*2 st v*2 st s pv s st v q s pv s*2 st*2 q st q s st s st k*2 "
        "s*2 st k s pv*2 m o*12",
        "s st s st z s k s q s q s st*2 k st s*2 k st q s st s st x st s pv*2 st s*2 st*2 s*2 st*2 s pv st*2 m x "
        "pv x*2",
        "x*2 s*2 st*2 x s st s st s st z s st s st pv s*2 st*2 q st s*2 pv st s q st*2 x q st pv s st s st k*3 s "
        "pv s m",
        "q*3 k*2 z st s st s st s st s st s st s st s st pv s st s st k s st*2 s pv s st s st s st s st pv s pv m",
    ),
    "act": (
        "v st*4 v*2 st*3 z st*2 v st*4 q st*2 split st norm k m gelu*4",
        "norm z st*5 k st*3 q x st*4 norm st*4 m norm x split x norm x norm",
        "x*2 norm st*6 x st z st norm st*4 x st q st*3 k m split",
        "q st*10 k st*4 z st*2 m split",
    ),
    "dve": (
        "s*6 rz*2 s rz ln s*4 rz ln s*2 cn s q s*2 k m res_add*2",
        "res_add s*2 res_add s rz s*2 rz s ln s*2 k s*2 ln s q x s*4 rz s ln*2 rz m cn x ln x*2",
        "x*2 s*5 ln s*2 x s*2 rz s rz s x s q rz s*2 rz s k s m cn",
        "q s*13 k s*3 rz m rz*3 cn",
    ),
    "pool": (
        "add*2 ln split ln add*4 ln*2",
        "add*3 ln*2 add ln add*2 split",
        "ln add*6 split",
        "add*6 split",
    ),
    "sp": (
        "res*2 load*2 rq rk shift store*2",
        "res*2 store*2 load*5 rk rq shift",
        "load rq rk shift",
        "rq shift rk",
    ),
}


def items(engine):
    steps, of_batch = [], {}
    for order in ORDER[engine]:
        of_step, step = {}, []
        for token in order.split():
            kind, _, times = token.partition("*")
            for _i in range(int(times or 1)):
                count = of_batch if kind in OVER_BATCH else of_step
                i = count.get(kind, 0)
                count[kind] = i + 1
                if kind in ("st", "s"):
                    step.append((kind, i // NC, i % NC))
                elif engine == "pe" and kind in ("q", "k", "v", "o"):
                    step.append((kind, i // PARTS, i % PARTS))
                else:
                    step.append((kind, i, 0))
        steps.append(step)
    return steps


PLAN = {engine: items(engine) for engine in ORDER}
for _n in range(2 * NC):
    for _s in range(NU):
        if ("x", _n, 0) in PLAN["pe"][_s]:
            assert _s > 1 or PLAN["pe"][_s].index(("x", _n, 0)) > PLAN["pe"][1].index(
                ("q" if _n < NC else "k", 0, PARTS - 1))
GEN = []
GEN_AT = {}
for _s in range(NU):
    for _kind, _n, _part in PLAN["pe"][_s]:
        if _part == 0 and _kind in ("v", "o", "x"):
            GEN_AT[(_kind, _s, _n)] = len(GEN)
            GEN.append((_kind, {"v": 0, "o": -1, "x": 1}[_kind], _n, 2 * NC if _kind == "x" else NC))
        if _part == 0 and _kind in ("q", "k", "m", "z"):
            _off = _s + {"q": 2, "k": 2, "m": 1, "z": -1}[_kind]
            GEN_AT[(_kind, _s, _off % NU)] = len(GEN)
            GEN.append((_kind, _off // NU, _off % NU, NU))
assert len(GEN) % 2 == 0


def build(nc, x, ctx_in, q_g, q_b, kv_g, kv_b, wq, wk, wv, wo, bo, out):
    B = x.shape[0]
    with ExitStack() as es:
        def sb(name, shape, dt=F32):
            return es.enter_context(nc.sbuf_tensor(name, shape, dt))

        def ps(name):
            return es.enter_context(nc.psum_tensor(name, [P, D], F32))

        def sem(name):
            return es.enter_context(nc.semaphore(name))

        w_hl = {n: sb(f"w_{n}", [P, 2, NC, D], F32R) for n in "qkvo"}
        q_stack = sb("q_stack", [P, 2, HU, D], F32R)
        k_stack = sb("k_stack", [P, 2, HU, D], F32R)
        q_nat = sb("q_nat", [P, 2, D], F32R)
        k_nat = sb("k_nat", [P, 2, D], F32R)
        xt = {"x": sb("xT", [P, 2, NC, D], F32R), "c": sb("cT", [P, 2, NC, D], F32R)}
        v_sb = sb("v_sb", [P, NC, D])
        probs = sb("probs", [P, NC, HU, D])
        ctx_hl = sb("ctx_hl", [P, 2, NU, D], F32R)
        ctx_n = sb("ctx_n", [P, D])
        tok = sb("tok", [P, NSLOT, D])
        rows = sb("rows", [P, D], F32R)
        ident = sb("ident", [P, P])
        ones = sb("ones", [P, DH])
        maxes = sb("maxes", [P, 2, HU * NC])
        stats = sb("stats", [P, 2, 6])
        moments = sb("moments", [P, 8, 2])
        neg_shift = sb("neg_shift", [P, 8])
        var_eps = sb("var_eps", [P, 8])
        rstd = sb("rstd", [P, 8])
        minus_half = sb("minus_half", [P, 1])
        minus_one = sb("minus_one", [P, 1])
        bias_q = sb("bias_q", [P, NU])
        bias_k = sb("bias_k", [P, NU])
        bias_nat = sb("bias_nat", [P, 3, NU])
        norm_cols = sb("norm_cols", [P, 4, NC])

        score = [ps(f"score{i}") for i in range(NC)]
        ctx_ps = [ps(f"ctx{i}") for i in range(2)]
        gen = [ps(f"gen{i}") for i in range(2)]

        full = {k: sem(f"{k}_in_psum") for k in "vomzxqk"}
        free = {k: sem(f"{k}_out_of_psum") for k in "vomzxqk"}
        st_full = sem("st_full")
        s_full = sem("s_full")
        exp_done = sem("exp_done")
        max_done = sem("max_done")
        pv_done = sem("pv_done")
        q_hi = sem("q_hi")
        k_hi = sem("k_hi")
        x_hi = sem("x_hi")
        m_hi = sem("m_hi")
        stack_used = sem("stack_used")
        q_stacked = sem("q_stacked")
        k_stacked = sem("k_stacked")
        shift_rows = sem("shift_rows")
        pool_added = sem("pool_added")
        ctx_read = sem("ctx_read")
        ctx_hi = sem("ctx_hi")
        ctx_split = sem("ctx_split")
        res_loaded = [sem(f"res_loaded{i}") for i in range(2)]
        res_added = sem("res_added")
        stored = [sem(f"stored{i}") for i in range(2)]
        tile_loaded = [sem(f"tile_loaded{i}") for i in range(8)]
        ln_stats = sem("ln_stats")
        ln_aggr = sem("ln_aggr")
        ln_var = sem("ln_var")
        ln_rstd = sem("ln_rstd")
        ln_done = sem("ln_done")
        ln_eps = sem("ln_eps")
        ln_shift = sem("ln_shift")
        z_inverted = sem("z_inverted")
        consts = sem("consts")
        w_loaded = sem("w_loaded")
        cols_loaded = sem("cols_loaded")
        bias_mm = sem("bias_mm")
        bias_cols = sem("bias_cols")
        bias_placed = sem("bias_placed")
        bo_mm = sem("bo_mm")
        bo_row = sem("bo_row")
        bo_hi = sem("bo_hi")
        bo_lo = sem("bo_lo")
        bo_placed = sem("bo_placed")
        w_scaled = sem("w_scaled")
        w_hi = sem("w_hi")
        w_ready = sem("w_ready")

        x_v = x.rearrange("b (i p) d -> (b i) p d", p=P)
        c_v = ctx_in.rearrange("b (i p) d -> (b i) p d", p=P)
        out_v = out.rearrange("b (i p) d -> (b i) p d", p=P)

        def known(b):
            return isinstance(b, int)

        def raw(ap):
            return ap.bitcast(F32)

        def valid(b):
            return not known(b) or 0 <= b < B

        def wait(eng, s, value):
            assert known(value) or value.min_val > 0
            if not known(value) or value > 0:
                eng.wait_ge(s, value)

        def unit(b, s, off):
            return b + (s + off) // NU, (s + off) % NU

        def place(kind, s, n):
            return GEN_AT[(kind, s, n)]

        def gen_at(kind, s, n):
            return gen[place(kind, s, n) % 2]

        def gen_bank(eng, b, kind, s, n):
            back = place(kind, s, n) - 2
            while back > -3 * len(GEN):
                kind2, off, n2, per = GEN[back % len(GEN)]
                b2 = b + off + back // len(GEN)
                if valid(b2):
                    wait(eng, free[kind2], b2 * per + n2 + 1)
                    break
                back -= 2
            return gen_at(kind, s, n)

        def by_head(name, ap):
            return ap.rearrange("p (u j d) -> p u j d", j=HU, d=DH) if name in "qk" else ap

        def by_dim(name, ap):
            return ap.rearrange("p (u d j) -> p u j d", j=HU, d=DH) if name in "qk" else ap

        def all_batches(eng, batch):
            batch(-1)
            batch(0)
            with eng.Fori(1, B - 1) as b:
                batch(b)
            batch(B - 1)
            batch(B)

        block = es.enter_context(nc.Block())

        @block.sync
        def _(sp):
            for n, w in enumerate((wo, wq, wk, wv)):
                sp.dma_start(probs[:, n], w.rearrange("(c p) n -> p c n", p=P)).then_inc(w_loaded, 16)
            sp.wait_ge(bias_cols, 3)
            for n, dst in enumerate((bias_q, bias_k)):
                for j in range(HU):
                    sp.dma_start(dst[j:P - HU + j + 1:HU, :],
                                 bias_nat[DH * j:DH * (j + 1), n, :]).then_inc(bias_placed, 16)
            sp.wait_ge(bo_lo, 1)
            for part in range(2):
                sp.dma_start(raw(rows[SROW + part:SROW + part + 1, :]),
                             raw(k_nat[0:1, part, :])).then_inc(bo_placed, 16)

            def load_tile(b, i):
                if i in (0, 1):
                    wait(sp, full["x"], 8 * (b - 1) + 6 + i)
                elif i in (2, 3):
                    if valid(b - 2):
                        wait(sp, stored[i - 2], 16 * (2 * (b - 2) + 2))
                    else:
                        wait(sp, full["x"], 8 * (b - 1) + (8 if i == 2 else 4))
                elif i == 4:
                    if valid(b - 2):
                        wait(sp, res_added, 4 * (b - 1))
                    else:
                        wait(sp, full["x"], 8 * (b - 1) + 5)
                else:
                    wait(sp, full["x"], 8 * b + i - 4)
                src = x_v[NC * b + i] if i < NC else c_v[NC * b + i - NC]
                sp.dma_start(tok[:, TILE_SLOT[i], :], src).then_inc(tile_loaded[i], 16)

            def load_residual(b, i):
                sp.dma_start(tok[:, i % 2, :], x_v[NC * b + i]).then_inc(res_loaded[i % 2], 16)

            def restack(u, nat, stack, parts, done):
                for third, part in enumerate(parts):
                    sp.dma_start(raw(stack[DH * third:DH * (third + 1), u % 2, :, :]),
                                 raw(nat[:, part, :])).then_inc(done, 16)

            def batch(b):
                for s in range(NU):
                    b1, u1 = unit(b, s, 1)
                    b2, u2 = unit(b, s, 2)
                    for kind, n, part in PLAN["sp"][s]:
                        if kind == "load" and valid(b + 1):
                            load_tile(b + 1, n)
                        if kind in ("rq", "rk") and valid(b2):
                            which = kind[1]
                            wait(sp, stack_used, NU * b2 + u2 + 1)
                            wait(sp, free[which], NU * b2 + u2 + 1)
                            if which == "q":
                                restack(u2, q_nat, q_stack, (0, 0, 1), q_stacked)
                            else:
                                restack(u2, k_nat, k_stack, (0, 1, 0), k_stacked)
                        if kind == "shift" and valid(b1):
                            wait(sp, free["m"], NU * b1 + u1 + 1)
                            for part2 in range(2):
                                sp.dma_start(
                                    raw(q_stack[SROW + part2:SROW + part2 + 1, u1 % 2, :, :].rearrange(
                                        "o h (c n) -> o (h c) n", n=P)),
                                    raw(rows[0:HU * NC, P * part2:P * (part2 + 1)])).then_inc(shift_rows, 16)
                        if kind == "res" and valid(b - 1):
                            if n < 2 and valid(b):
                                wait(sp, full["x"], 8 * b + 8)
                            else:
                                wait(sp, stored[n % 2], 16 * (2 * (b - 1) + n // 2))
                            load_residual(b - 1, n)
                        if kind == "store" and valid(b - 1):
                            wait(sp, res_added, 4 * (b - 1) + n + 1)
                            sp.dma_start(out_v[NC * (b - 1) + n], tok[:, n % 2, :]).then_inc(stored[n % 2], 16)

            all_batches(sp, batch)
            for i in range(2):
                sp.wait_ge(stored[i], 16 * 2 * B)

        @block.gpsimd
        def _(pool):
            pool.memset(ident[:], 0.0).then_inc(consts, 1)
            pool.memset(ones[:], 1.0).then_inc(consts, 1)
            pool.memset(minus_half[:], -0.5).then_inc(consts, 1)
            pool.wait_ge(consts, 3)
            pool.memset(raw(k_stack[SROW:SROW + 2, :, :, :]), 1.0).then_inc(consts, 1)
            pool.wait_ge(consts, 4)
            pool.affine_select(out=ident[:], in_=ident[:], compare_op=ALU.not_equal, fill=1.0, base=0,
                               pattern=[[-1, P]], channel_multiplier=1).then_inc(consts, 1)

            def add(t, n):
                c, half = n // 2, n % 2
                heads = slice(HU // 2 * half, HU // 2 * (half + 1))
                wait(pool, exp_done, 16 * t + HU * (c + 1) + 2 * (half + 1))
                wait(pool, pv_done, 4 * t + c + 2)
                if c > 0:
                    wait(pool, pool_added, 6 * t + n - 1)
                pool.tensor_tensor(probs[:, c + 1, heads], probs[:, c + 1, heads], probs[:, c, heads],
                                   ALU.add).then_inc(pool_added, 1)

            def batch(b):
                for s in range(NU):
                    bp, up = unit(b, s, -1)
                    for kind, n, part in PLAN["pool"][s]:
                        if kind == "add" and valid(b):
                            add(NU * b + s, n)
                        if kind == "ln" and valid(b + 1):
                            k = 8 * (b + 1) + n
                            wait(pool, ln_var, k + 1)
                            wait(pool, ln_done, k - 7)
                            pool.tensor_tensor(rstd[:, n:n + 1], var_eps[:, n:n + 1], minus_half[:],
                                               ALU.pow).then_inc(ln_rstd, 1)
                            wait(pool, ln_rstd, k + 1)
                            pool.tensor_tensor(neg_shift[:, n:n + 1], moments[:, n, 0:1], rstd[:, n:n + 1],
                                               ALU.mult).then_inc(ln_shift, 1)
                        if kind == "split" and valid(bp):
                            wait(pool, ctx_hi, NU * bp + up + 1)
                            pool.tensor_tensor(ctx_hl[:, 1, up], ctx_n[:], raw(ctx_hl[:, 0, up]),
                                               ALU.subtract).then_inc(ctx_split, 1)

            all_batches(pool, batch)

        @block.scalar
        def _(act):
            for n, col in enumerate((q_g, q_b, kv_g, kv_b)):
                act.dma_start(norm_cols[:, n, :], col.rearrange("(c p) -> p c", p=P),
                              allow_slow_non_contiguous=True).then_inc(cols_loaded, 16)
            act.dma_start(ctx_n[0:1, :], bo.rearrange("(a n) -> a n", a=1)).then_inc(cols_loaded, 16)
            act.wait_ge(w_loaded, 16 * 4)
            for n, name in enumerate("oqkv"):
                for c in range(NC):
                    if n > 0:
                        act.wait_ge(w_scaled, NC * (n - 1) + c + 1)
                    act.activation(by_dim(name, w_hl[name][:, 0, c, :]), by_head(name, probs[:, n, c, :]),
                                   ACT.Identity).then_inc(w_hi, 1)
            act.wait_ge(bo_row, 1)
            act.activation(k_nat[0:1, 0, :], ctx_n[0:1, :], ACT.Identity).then_inc(bo_hi, 1)
            act.wait_ge(bo_placed, 32)
            act.wait_ge(bias_placed, 16 * 2 * HU)

            def batch(b):
                for s in range(NU):
                    t = NU * b + s
                    b1, u1 = unit(b, s, 1)
                    b2, u2 = unit(b, s, 2)
                    bp, up = unit(b, s, -1)
                    for kind, n, part in PLAN["act"][s]:
                        if kind == "st" and valid(b):
                            if n < 3 and part % 2 == 0:
                                wait(act, pool_added, 6 * (t - 1) + 2 * n + part // 2 + 1)
                            if n == 3 and part == 0:
                                wait(act, full["z"], t)
                            i = HU * n + part
                            wait(act, st_full, 16 * t + i + 1)
                            act.activation(probs[:, n, part, :], score[i % 2][:], ACT.Exp,
                                           scale=SCALE).then_inc(exp_done, 1)
                        if kind == "z" and valid(bp):
                            wait(act, full["z"], NU * bp + up + 1)
                            wait(act, ctx_split, NU * bp + up)
                            act.activation(ctx_n[:], gen_at("z", s, up)[:], ACT.Identity).then_inc(free["z"], 1)
                        if kind == "split" and valid(bp):
                            wait(act, ctx_read, NU * bp + up + 1)
                            if up == 0:
                                wait(act, full["o"], NC * b)
                            act.activation(ctx_hl[:, 0, up, :], ctx_n[:], ACT.Identity).then_inc(ctx_hi, 1)
                        if kind == "v" and valid(b):
                            wait(act, full["v"], 4 * b + n + 1)
                            act.activation(v_sb[:, n, :], gen_at("v", s, n)[:], ACT.Identity).then_inc(free["v"], 1)
                        if kind == "gelu" and valid(b - 1):
                            wait(act, full["o"], 4 * (b - 1) + n + 1)
                            if n == 0 and valid(b):
                                wait(act, full["x"], 8 * b + 5)
                            else:
                                wait(act, res_added, 4 * (b - 1) + n)
                            act.activation(tok[:, 2, :], gen_at("o", s, n)[:], ACT.Gelu).then_inc(free["o"], 1)
                        if kind == "norm" and valid(b + 1):
                            tile = tok[:, TILE_SLOT[n], :]
                            wait(act, ln_shift, 8 * (b + 1) + n + 1)
                            act.activation(tile, tile, ACT.Identity, bias=neg_shift[:, n:n + 1],
                                           scale=rstd[:, n:n + 1]).then_inc(ln_done, 1)
                        if kind == "x" and valid(b + 1):
                            wait(act, full["x"], 8 * (b + 1) + n + 1)
                            act.activation(xt["x" if n < NC else "c"][:, 0, :, P * (n % NC):P * (n % NC + 1)],
                                           gen_at("x", s, n)[:].rearrange("p (c n) -> p c n", c=NC),
                                           ACT.Identity).then_inc(x_hi, 1)
                        if kind == "q" and valid(b2):
                            wait(act, full["q"], NU * b2 + u2 + 1)
                            wait(act, q_stacked, 48 * (NU * b2 + u2))
                            act.activation(q_nat[:, 0, :], gen_at("q", s, u2)[:], ACT.Identity,
                                           bias=bias_q[:, u2:u2 + 1]).then_inc(q_hi, 1)
                        if kind == "k" and valid(b2):
                            wait(act, full["k"], NU * b2 + u2 + 1)
                            wait(act, k_stacked, 48 * (NU * b2 + u2))
                            act.activation(k_nat[:, 0, :], gen_at("k", s, u2)[:], ACT.Identity,
                                           bias=bias_k[:, u2:u2 + 1]).then_inc(k_hi, 1)
                        if kind == "m" and valid(b1):
                            wait(act, full["m"], NU * b1 + u1 + 1)
                            wait(act, shift_rows, 32 * (NU * b1 + u1))
                            act.activation(rows[0:HU * NC, 0:P], gen_at("m", s, u1)[0:HU * NC, 0:P],
                                           ACT.Identity).then_inc(m_hi, 1)

            all_batches(act, batch)

        @block.vector
        def _(dve):
            dve.memset(minus_one[:], -1.0).then_inc(stack_used, 2)
            dve.wait_ge(cols_loaded, 16 * 5)
            dve.wait_ge(w_loaded, 16 * 4)

            def low_weights(n, name):
                for c in range(NC):
                    dve.wait_ge(w_hi, NC * n + c + 1)
                    dve.tensor_tensor(by_dim(name, w_hl[name][:, 1, c, :]), by_head(name, probs[:, n, c, :]),
                                      by_dim(name, raw(w_hl[name][:, 0, c, :])), ALU.subtract).then_inc(w_ready, 1)

            low_weights(0, "o")
            for n, (name, gain) in enumerate((("q", 0), ("k", 2), ("v", 2))):
                dve.wait_ge(bias_mm, n + 1)
                dve.tensor_copy(bias_nat[:, n, :], score[n][:, 0:NU]).then_inc(bias_cols, 1)
                for c in range(NC):
                    w = probs[:, n + 1, c, :]
                    dve.tensor_scalar(w, w, norm_cols[:, gain, c:c + 1], None, ALU.mult).then_inc(w_scaled, 1)
                low_weights(n + 1, name)
            dve.wait_ge(bo_mm, 1)
            dve.tensor_tensor(ctx_n[0:1, :], score[3][0:1, :], ctx_n[0:1, :], ALU.add).then_inc(bo_row, 1)
            dve.wait_ge(bo_hi, 1)
            dve.tensor_tensor(k_nat[0:1, 1, :], ctx_n[0:1, :], raw(k_nat[0:1, 0, :]), ALU.subtract).then_inc(bo_lo, 1)

            dve.wait_ge(bias_placed, 16 * 2 * HU)

            def moments_of(b, n):
                k = 8 * b + n
                wait(dve, tile_loaded[n], 16 * (b + 1))
                dve.bn_stats(stats[:, n % 2, :], tok[:, TILE_SLOT[n], :]).then_inc(ln_stats, 1)
                wait(dve, ln_rstd, k - 7)
                dve.memset(var_eps[:, n:n + 1], EPS).then_inc(ln_eps, 1)
                wait(dve, ln_stats, k + 1)
                wait(dve, ln_shift, k - 7)
                dve.memset(minus_one[:], -1.0).then_inc(ln_eps, 1)
                dve.bn_aggr(moments[:, n, :], stats[:, n % 2, :]).then_inc(ln_aggr, 1)
                wait(dve, ln_aggr, k + 1)
                wait(dve, ln_eps, 2 * k + 2)
                dve.tensor_tensor(var_eps[:, n:n + 1], moments[:, n, 1:2], var_eps[:, n:n + 1], ALU.add)
                dve.tensor_tensor(moments[:, n, 0:1], moments[:, n, 0:1], minus_one[:], ALU.mult).then_inc(ln_var, 1)

            def low_part(dst, psum, hi, done, bias=None):
                if bias is None:
                    dve.tensor_tensor(dst, psum, raw(hi), ALU.subtract).then_inc(done, 1)
                else:
                    dve.scalar_tensor_tensor(out=dst, in0=psum, scalar=bias, in1=raw(hi), op0=ALU.add,
                                             op1=ALU.subtract).then_inc(done, 1)

            def batch(b):
                for s in range(NU):
                    b1, u1 = unit(b, s, 1)
                    b2, u2 = unit(b, s, 2)
                    bp, up = unit(b, s, -1)
                    t1, t2, tp = NU * b1 + u1, NU * b2 + u2, NU * bp + up
                    for kind, n, part in PLAN["dve"][s]:
                        if kind == "s" and valid(b1):
                            i = NC * n + part
                            if i == 0:
                                wait(dve, full["m"], t1 - 1)
                            wait(dve, s_full, 16 * t1 + i + 1)
                            dve.tensor_reduce(maxes[:, u1 % 2, i:i + 1], score[2 + i % 2][:], AX_X, ALU.max,
                                              negate=True).then_inc(max_done, 1)
                        if kind == "rz" and valid(bp):
                            if n == 0:
                                wait(dve, free["z"], tp + 1)
                            cols = slice(P * n, P * (n + 1))
                            dve.reciprocal(ctx_n[:, cols], ctx_n[:, cols]).then_inc(z_inverted, 1)
                        if kind == "cn" and valid(bp):
                            wait(dve, z_inverted, 4 * tp + 4)
                            wait(dve, pv_done, 4 * tp + 4)
                            dve.tensor_tensor(ctx_n[:], ctx_ps[up % 2][:], ctx_n[:], ALU.mult).then_inc(ctx_read, 1)
                        if kind == "ln" and valid(b + 1):
                            moments_of(b + 1, n)
                        if kind == "res_add" and valid(b - 1):
                            wait(dve, free["o"], 4 * (b - 1) + n + 1)
                            wait(dve, res_loaded[n % 2], 16 * (2 * (b - 1) + n // 2 + 1))
                            dve.tensor_tensor(tok[:, n % 2], tok[:, n % 2], tok[:, 2], ALU.add).then_inc(res_added, 1)
                        if kind == "x" and valid(b + 1):
                            src = xt["x" if n < NC else "c"]
                            cols = slice(P * (n % NC), P * (n % NC + 1))
                            wait(dve, x_hi, 8 * (b + 1) + n + 1)
                            low_part(src[:, 1, :, cols], gen_at("x", s, n)[:].rearrange("p (c n) -> p c n", c=NC),
                                     src[:, 0, :, cols], free["x"])
                        if kind == "q" and valid(b2):
                            wait(dve, q_hi, t2 + 1)
                            low_part(q_nat[:, 1, :], gen_at("q", s, u2)[:], q_nat[:, 0, :], free["q"],
                                     bias_q[:, u2:u2 + 1])
                        if kind == "k" and valid(b2):
                            wait(dve, k_hi, t2 + 1)
                            low_part(k_nat[:, 1, :], gen_at("k", s, u2)[:], k_nat[:, 0, :], free["k"],
                                     bias_k[:, u2:u2 + 1])
                        if kind == "m" and valid(b1):
                            wait(dve, m_hi, t1 + 1)
                            low_part(rows[0:HU * NC, P:2 * P], gen_at("m", s, u1)[0:HU * NC, 0:P],
                                     rows[0:HU * NC, 0:P], free["m"])

            all_batches(dve, batch)

        @block.tensor
        def _(pe):
            pe.wait_ge(consts, 5)
            pe.wait_ge(cols_loaded, 16 * 5)
            pe.wait_ge(w_loaded, 16 * 4)
            for n, shift in enumerate((1, 3, 3)):
                for u in range(NU):
                    for c in range(NC):
                        mm = pe.matmul(score[n][:, u:u + 1], probs[:, n + 1, c, P * u:P * (u + 1)],
                                       norm_cols[:, shift, c:c + 1], start=(c == 0), stop=(c == NC - 1))
                mm.then_inc(bias_mm, 1)
            pe.wait_ge(bias_cols, 3)
            for u in range(NU):
                mm = pe.matmul(score[3][0:1, :], bias_nat[:, 2, u:u + 1], probs[:, 0, u, :], start=(u == 0),
                               stop=(u == NU - 1))
            mm.then_inc(bo_mm, 1)
            pe.wait_ge(w_ready, 16)
            pe.wait_ge(bo_placed, 32)

            def product(bank, stationary, moving, part, closed=True):
                hs, hm = ((0, 0), (0, 1), (1, 0))[part]
                for c in range(NC):
                    mm = pe.matmul(bank[:, :], stationary(hs, c), moving(hm, c), start=(part == 0 and c == 0),
                                   stop=(closed and part == PARTS - 1 and c == NC - 1))
                return mm

            def batch(b):
                for s in range(NU):
                    b1, u1 = unit(b, s, 1)
                    b2, u2 = unit(b, s, 2)
                    bp, up = unit(b, s, -1)
                    t, t1, t2, tp = NU * b + s, NU * b1 + u1, NU * b2 + u2, NU * bp + up
                    for kind, n, part in PLAN["pe"][s]:
                        if kind == "st" and valid(b):
                            i = HU * n + part
                            if i == 0:
                                wait(pe, shift_rows, 32 * (t + 1))
                            wait(pe, exp_done, 16 * t + i - 1)
                            pe.matmul(score[i % 2][:, :], k_stack[0:SROW + 2, s % 2, part, P * n:P * (n + 1)],
                                      q_stack[0:SROW + 2, s % 2, part, :], start=True, stop=True).then_inc(st_full, 1)
                        if kind == "s" and valid(b1):
                            i = NC * n + part
                            if i == 0:
                                wait(pe, q_stacked, 48 * (t1 + 1))
                                wait(pe, k_stacked, 48 * (t1 + 1))
                            wait(pe, max_done, 16 * t1 + i - 1)
                            pe.matmul(score[2 + i % 2][:, :], q_stack[0:KROWS, u1 % 2, n, P * part:P * (part + 1)],
                                      k_stack[0:KROWS, u1 % 2, n, :], start=True, stop=True).then_inc(s_full, 1)
                        if kind == "pv" and valid(b):
                            wait(pe, exp_done, 16 * t + 4 * n + 4)
                            if n == 0:
                                wait(pe, ctx_read, t - 1)
                            if s == 0:
                                wait(pe, free["v"], 4 * b + n + 1)
                            for j in range(HU):
                                lo = P * s + DH * j
                                mm = pe.matmul(ctx_ps[s % 2][DH * j:DH * (j + 1), :], v_sb[:, n, lo:lo + DH],
                                               probs[:, n, j, :], start=(n == 0), stop=(n == NC - 1))
                                if n == NC - 1 and j == 0:
                                    mm.then_inc(stack_used, 1)
                            mm.then_inc(pv_done, 1)
                        if kind == "z" and valid(bp):
                            bank = gen_bank(pe, b, "z", s, up)
                            wait(pe, pool_added, 6 * tp + 6)
                            for j in range(HU):
                                mm = pe.matmul(bank[DH * j:DH * (j + 1), :], ones[:], probs[:, 3, j, :], start=True,
                                               stop=True)
                            mm.then_inc(full["z"], 1)
                        if kind == "v" and valid(b):
                            bank = gen_bank(pe, b, "v", s, n) if part == 0 else gen_at("v", s, n)
                            mm = product(bank, lambda h, c: xt["c"][:, h, c, P * n:P * (n + 1)],
                                         lambda h, c: w_hl["v"][:, h, c, :], part)
                            if part == PARTS - 1:
                                mm.then_inc(full["v"], 1)
                        if kind == "o" and valid(b - 1):
                            if n == 0 and part == 0:
                                wait(pe, ctx_split, NU * b)
                            bank = gen_bank(pe, b, "o", s, n) if part == 0 else gen_at("o", s, n)
                            product(bank, lambda h, c: ctx_hl[:, h, c, P * n:P * (n + 1)],
                                    lambda h, c: w_hl["o"][:, h, c, :], part, closed=False)
                            if part == PARTS - 1:
                                pe.matmul(bank[:, :], k_stack[SROW:SROW + 2, 0, 0, 0:P], rows[SROW:SROW + 2, :],
                                          start=False, stop=True).then_inc(full["o"], 1)
                        if kind == "x" and valid(b + 1):
                            bank = gen_bank(pe, b, "x", s, n)
                            wait(pe, ln_done, 8 * (b + 1) + n + 1)
                            for c in range(NC):
                                mm = pe.matmul(bank[:, P * c:P * (c + 1)],
                                               tok[:, TILE_SLOT[n], P * c:P * (c + 1)], ident[:], start=True,
                                               stop=True, is_transpose=True)
                            mm.then_inc(full["x"], 1)
                        if kind in ("q", "k") and valid(b2):
                            bank = gen_bank(pe, b, kind, s, u2) if part == 0 else gen_at(kind, s, u2)
                            if part == 0 and u2 == 0:
                                wait(pe, free["x"], 8 * b2 + (NC if kind == "q" else 2 * NC))
                            src = xt["x" if kind == "q" else "c"]
                            mm = product(bank, lambda h, c: w_hl[kind][:, h, c, P * u2:P * (u2 + 1)],
                                         lambda h, c: src[:, h, c, :], part)
                            if part == PARTS - 1:
                                mm.then_inc(full[kind], 1)
                        if kind == "m" and valid(b1):
                            bank = gen_bank(pe, b, "m", s, u1)
                            wait(pe, max_done, 16 * (t1 + 1))
                            pe.matmul(bank[0:HU * NC, 0:P], maxes[:, u1 % 2, :], ident[:], start=True, stop=True,
                                      is_transpose=True).then_inc(full["m"], 1)

            all_batches(pe, batch)


_INS = ["x", "ctx_1024", "L0_xattn_q_norm_g", "L0_xattn_q_norm_b", "L0_xattn_kv_norm_g", "L0_xattn_kv_norm_b",
        "L0_xattn_Wq", "L0_xattn_Wk", "L0_xattn_Wv", "L0_xattn_Wo", "L0_xattn_bo"]


def kernel(**inputs):
    import numpy as np
    import concourse.bacc as bacc
    from concourse.bass_utils import run_bass_kernel_spmd

    nc = bacc.Bacc("TRN2", target_bir_lowering=False, num_devices=1)
    arrays, args = {}, []
    for name in _INS:
        a = np.ascontiguousarray(inputs[name])
        arrays[f"in_{name}"] = a
        args.append(nc.dram_tensor(f"in_{name}", a.shape, mybir.dt.from_np(a.dtype), kind="ExternalInput").ap())
    shape = arrays["in_x"].shape
    args.append(nc.dram_tensor("out_0", shape, F32, kind="ExternalOutput").ap())
    build(nc, *args)
    r = run_bass_kernel_spmd(nc, [arrays], core_ids=[0])
    return r.results[0]["out_0"]
```
